# Optimizing a Trainium2 kernel written in Bass

```python
import numpy as np
import jax
import jax.numpy as jnp

def _softmax(x, axis=-1):
    return jax.nn.softmax(x, axis=axis)

def _gelu(x):
    return jax.nn.gelu(x, approximate=True)

def _silu(x):
    return jax.nn.silu(x)

def _sigmoid(x):
    return jax.nn.sigmoid(x)

def _layernorm(x, axis=-1, eps=1e-05):
    m = jnp.mean(x, axis=axis, keepdims=True)
    v = jnp.var(x, axis=axis, keepdims=True)
    return (x - m) / jnp.sqrt(v + eps)

def _scatter_add(tgt, idx, src, axis=0):
    return tgt.at[idx].add(src)

def _segment_sum(src, seg, n):
    return jax.ops.segment_sum(src, seg, n)
kernel_name = 'mk_gnn_resnorm_d4_gnn_r8_0df0b2'

def setup_inputs(seed: int=0):
    np.random.seed(seed)
    _w = jnp.asarray

    def _rec_inputs():
        import jax
        import jax.numpy as jnp
        _gk = jax.random.key(seed)
        x = -0.0001006 + 1 * jax.random.normal(jax.random.fold_in(_gk, 1), (12500, 48), jnp.float32)
        src = jax.random.randint(jax.random.fold_in(_gk, 2), (400000,), 0, 12500, jnp.int32)
        dst = jax.random.randint(jax.random.fold_in(_gk, 3), (400000,), 0, 12500, jnp.int32)
        _o = jnp.argsort(dst, stable=True)
        src = src[_o]
        dst = dst[_o]
        edge_attr_32 = 0.000189758 + 1.00013 * jax.random.normal(jax.random.fold_in(_gk, 13), (400000, 32), jnp.float32)
        edge_attr_40 = jax.random.uniform(jax.random.fold_in(_gk, 14), (400000, 40), jnp.float32, 0.0, 1)
        edge_weight = jax.random.uniform(jax.random.fold_in(_gk, 16), (400000,), jnp.float32, 0.0, 6.99999)
        node_type_119 = jax.random.randint(jax.random.fold_in(_gk, 17), (12500,), 0, 119, jnp.int32)
        node_vec = jax.random.uniform(jax.random.fold_in(_gk, 18), (12500,), jnp.float32, 0.0, 1.49999)
        return (x, src, dst, edge_attr_32, edge_attr_40, edge_weight, node_type_119, node_vec)
    x, src, dst, edge_attr_32, edge_attr_40, edge_weight, node_type_119, node_vec = _rec_inputs()

    def _L0_gnn_setup():
        import jax, jax.numpy as jnp
        import numpy as np
        N_NODES = 12500
        key = jax.random.key(seed)
        k1, k2, k3, k4, k5, k6 = jax.random.split(key, 6)
        node_dim, edge_dim, hidden = (48, 32, 128)
        E = 200000
        x = jax.random.normal(k1, (N_NODES, node_dim), dtype=jnp.float32)
        edge_index = jax.random.randint(k2, (2, E), 0, N_NODES, dtype=jnp.int64)
        edge_attr = jax.random.normal(k3, (E, edge_dim), dtype=jnp.float32)
        in_dim = 2 * node_dim + edge_dim
        s1 = 1.0 / np.sqrt(in_dim)
        s2 = 1.0 / np.sqrt(hidden)
        W1 = jax.random.uniform(k4, (in_dim, hidden), minval=-s1, maxval=s1, dtype=jnp.float32)
        b1 = jax.random.uniform(k5, (hidden,), minval=-s1, maxval=s1, dtype=jnp.float32)
        W2 = jax.random.uniform(k6, (hidden, node_dim), minval=-s2, maxval=s2, dtype=jnp.float32)
        b2 = jnp.zeros((node_dim,), dtype=jnp.float32)
        return {'x': x, 'edge_index': edge_index, 'edge_attr': edge_attr, 'W1': W1, 'b1': b1, 'W2': W2, 'b2': b2}
    _L0_gnn_all = _L0_gnn_setup()
    _L0_gnn_in = {k: v for k, v in _L0_gnn_all.items() if k in ('W1', 'b1', 'W2', 'b2')}
    del _L0_gnn_all

    def _L1_gnn_setup():
        import jax, jax.numpy as jnp
        import numpy as np
        N_NODES = 6250
        N_EDGES = 200000
        D_IN = 48
        D_OUT = 48
        key = jax.random.key(seed)
        k1, k2, k3, k4 = jax.random.split(key, 4)
        features = jax.random.normal(k1, (N_NODES, D_IN), dtype=jnp.float32)
        src = jax.random.randint(k2, (N_EDGES,), 0, N_NODES, dtype=jnp.int64)
        dst = jax.random.randint(k3, (N_EDGES,), 0, N_NODES, dtype=jnp.int64)
        std = np.sqrt(2.0 / (D_IN + D_OUT))
        W = jax.random.normal(k4, (D_OUT, D_IN), dtype=jnp.float32) * std
        b = jnp.zeros((D_OUT,), dtype=jnp.float32)
        return {'features': features, 'src': src, 'dst': dst, 'W': W, 'b': b}
    _L1_gnn_all = _L1_gnn_setup()
    _L1_gnn_in = {k: v for k, v in _L1_gnn_all.items() if k in ('W', 'b')}
    del _L1_gnn_all

    def _L2_gnn_setup():
        import jax, jax.numpy as jnp
        import numpy as np
        N_NODES = 12500
        N_EDGES = 200000
        IN_F = 48
        OUT_F = 48
        key = jax.random.key(seed)
        k1, k2, k3, k4 = jax.random.split(key, 4)
        x = jax.random.normal(k1, (N_NODES, IN_F), dtype=jnp.float32)
        edge_index = jax.random.randint(k2, (2, N_EDGES), 0, N_NODES, dtype=jnp.int32)
        bound = 1.0 / np.sqrt(IN_F)
        W = jax.random.uniform(k3, (OUT_F, IN_F), minval=-bound, maxval=bound, dtype=jnp.float32)
        b = jax.random.uniform(k4, (OUT_F,), minval=-bound, maxval=bound, dtype=jnp.float32)
        return {'x': x, 'edge_index': edge_index, 'W': W, 'b': b}
    _L2_gnn_all = _L2_gnn_setup()
    _L2_gnn_in = {k: v for k, v in _L2_gnn_all.items() if k in ('W', 'b')}
    del _L2_gnn_all

    def _L3_gnn_setup():
        import jax, jax.numpy as jnp
        import numpy as np
        CUTOFF = 6.0
        LN_EPS = 1e-05
        key = jax.random.key(seed)
        ks = jax.random.split(key, 16)
        N, E, H, R, NEL, G = (6250, 100000, 48, 40, 119, 32)
        inp = {'h': jax.random.normal(ks[0], (N, H), jnp.float32), 'edge_index': jax.random.randint(ks[1], (2, E), 0, N, jnp.int64), 'edge_attr': jax.random.uniform(ks[2], (E, R), jnp.float32), 'distances': jax.random.uniform(ks[3], (E,), jnp.float32) * 7.0, 'atom_z': jax.random.randint(ks[4], (N,), 0, NEL, jnp.int64), 'node_mult': jax.random.uniform(ks[5], (N,), jnp.float32) + 0.5, 'batch': jnp.zeros((N,), jnp.int64), 'W1': jax.random.normal(ks[6], (H, R), jnp.float32) / np.sqrt(R), 'b1': jax.random.normal(ks[7], (H,), jnp.float32) * 0.01, 'W2': jax.random.normal(ks[8], (H, H), jnp.float32) / np.sqrt(H), 'b2': jax.random.normal(ks[9], (H,), jnp.float32) * 0.01, 'emb': jax.random.normal(ks[10], (NEL, G), jnp.float32) * 0.01, 'adaptW': jax.random.normal(ks[11], (G, G), jnp.float32) * 0.01, 'gamma': jnp.ones((H,), jnp.float32), 'beta': jnp.zeros((H,), jnp.float32)}
        return inp
    _L3_gnn_all = _L3_gnn_setup()
    _L3_gnn_in = {k: v for k, v in _L3_gnn_all.items() if k in ('W1', 'b1', 'W2', 'b2', 'emb', 'adaptW', 'gamma', 'beta')}
    del _L3_gnn_all
    return {'x': x, 'src': src, 'dst': dst, 'edge_attr_32': edge_attr_32, 'edge_attr_40': edge_attr_40, 'edge_weight': edge_weight, 'node_type_119': node_type_119, 'node_vec': node_vec, 'L0_gnn_W1': _L0_gnn_in['W1'], 'L0_gnn_b1': _L0_gnn_in['b1'], 'L0_gnn_W2': _L0_gnn_in['W2'], 'L0_gnn_b2': _L0_gnn_in['b2'], 'L1_gnn_W': _L1_gnn_in['W'], 'L1_gnn_b': _L1_gnn_in['b'], 'L2_gnn_W': _L2_gnn_in['W'], 'L2_gnn_b': _L2_gnn_in['b'], 'L3_gnn_W1': _L3_gnn_in['W1'], 'L3_gnn_b1': _L3_gnn_in['b1'], 'L3_gnn_W2': _L3_gnn_in['W2'], 'L3_gnn_b2': _L3_gnn_in['b2'], 'L3_gnn_emb': _L3_gnn_in['emb'], 'L3_gnn_adaptW': _L3_gnn_in['adaptW'], 'L3_gnn_gamma': _L3_gnn_in['gamma'], 'L3_gnn_beta': _L3_gnn_in['beta']}

def reference(x, src, dst, edge_attr_32, edge_attr_40, edge_weight, node_type_119, node_vec, L0_gnn_W1, L0_gnn_b1, L0_gnn_W2, L0_gnn_b2, L1_gnn_W, L1_gnn_b, L2_gnn_W, L2_gnn_b, L3_gnn_W1, L3_gnn_b1, L3_gnn_W2, L3_gnn_b2, L3_gnn_emb, L3_gnn_adaptW, L3_gnn_gamma, L3_gnn_beta):
    import jax
    import jax.numpy as jnp

    def _L0_gnn_ref(x, edge_index, edge_attr, W1, b1, W2, b2):
        import jax, jax.numpy as jnp
        import numpy as np
        N_NODES = 12500
        src, dst = (edge_index[0], edge_index[1])
        x_i = x[dst]
        x_j = x[src]
        tmp = jnp.concatenate([x_i, x_j, edge_attr], axis=1)
        h = jax.nn.relu(tmp @ W1 + b1)
        msg = h @ W2 + b2
        out = jax.ops.segment_sum(msg, dst, num_segments=N_NODES)
        return out

    def _L1_gnn_ref(features, src, dst, W, b):
        import jax, jax.numpy as jnp
        import numpy as np
        N_NODES = 6250
        N_EDGES = 200000
        D_IN = 48
        D_OUT = 48
        n = features.shape[0]
        ones = jnp.ones(src.shape[0], dtype=features.dtype)
        out_deg = jax.ops.segment_sum(ones, src, num_segments=n)
        in_deg = jax.ops.segment_sum(ones, dst, num_segments=n)
        ci = jax.lax.rsqrt(jnp.maximum(out_deg, 1.0))
        cj = jax.lax.rsqrt(jnp.maximum(in_deg, 1.0))
        msg = features[src] * ci[src][:, None]
        agg = jax.ops.segment_sum(msg, dst, num_segments=n) * cj[:, None]
        h = jnp.where(in_deg[:, None] > 0, agg, features)
        out = jax.nn.relu(h @ W.T + b)
        return out

    def _L2_gnn_ref(x, edge_index, W, b):
        import jax, jax.numpy as jnp
        import numpy as np
        N_NODES = 12500
        N_EDGES = 200000
        IN_F = 48
        OUT_F = 48
        row, col = (edge_index[0], edge_index[1])
        n = x.shape[0]
        deg = jnp.bincount(row, length=n).astype(x.dtype)
        deg_inv_sqrt = jnp.where(deg > 0, jax.lax.rsqrt(jnp.where(deg > 0, deg, 1.0)), 0.0)
        norm = deg_inv_sqrt[row] * deg_inv_sqrt[col]
        msg = norm[:, None] * x[col]
        agg = jax.ops.segment_sum(msg, row, num_segments=n)
        out = agg @ W.T + b
        return jax.nn.relu(out)

    def _L3_gnn_ref(h, edge_index, edge_attr, distances, atom_z, node_mult, batch, W1, b1, W2, b2, emb, adaptW, gamma, beta):
        import jax, jax.numpy as jnp
        import numpy as np
        CUTOFF = 6.0
        LN_EPS = 1e-05
        src, dst = (edge_index[0], edge_index[1])
        N = h.shape[0]
        gate = jax.nn.silu(edge_attr @ W1.T + b1) @ W2.T + b2
        ei = emb[atom_z[src]]
        ej = emb[atom_z[dst]]
        adapt_logit = jnp.sum(ei * (ej @ adaptW.T), axis=-1, keepdims=True)
        gate = gate + adapt_logit
        cw = jnp.where(distances < CUTOFF, 0.5 * (jnp.cos(jnp.pi * distances / CUTOFF) + 1.0), 0.0)
        mj = node_mult[dst]
        msg = gate * h[dst] * (cw * mj)[:, None]
        agg = jax.ops.segment_sum(msg, src, num_segments=N)
        tot = jax.ops.segment_sum(mj, src, num_segments=N)
        agg = agg / jnp.clip(tot, 1e-08, None)[:, None]
        x = h + agg
        mu = jnp.mean(x, axis=-1, keepdims=True)
        var = jnp.mean(jnp.square(x - mu), axis=-1, keepdims=True)
        return (x - mu) / jnp.sqrt(var + LN_EPS) * gamma + beta
    edge_index = jnp.stack([src, dst])
    batch0 = jnp.zeros((12500,), jnp.int32)
    x = _layernorm(x + _L0_gnn_ref(x, edge_index, edge_attr_32, L0_gnn_W1, L0_gnn_b1, L0_gnn_W2, L0_gnn_b2), axis=-1)
    x = _layernorm(x + _L1_gnn_ref(x, src, dst, L1_gnn_W, L1_gnn_b), axis=-1)
    x = _layernorm(x + _L2_gnn_ref(x, edge_index, L2_gnn_W, L2_gnn_b), axis=-1)
    x = _layernorm(x + _L3_gnn_ref(x, edge_index, edge_attr_40, edge_weight, node_type_119, node_vec, batch0, L3_gnn_W1, L3_gnn_b1, L3_gnn_W2, L3_gnn_b2, L3_gnn_emb, L3_gnn_adaptW, L3_gnn_gamma, L3_gnn_beta), axis=-1)
    return x

_drawn_inputs = setup_inputs


def setup_inputs(seed=0):
    import zlib

    import numpy as np

    out = dict(_drawn_inputs(seed))
    spreads = {'L0_gnn_b2': (0.0, 0.1),
     'L1_gnn_b': (0.0, 0.1),
     'L3_gnn_gamma': (1.0, 0.2),
     'L3_gnn_beta': (0.0, 0.1)}
    factors = {'edge_attr_40': 5.424,
     'edge_weight': 4.697,
     'node_vec': 7.341,
     'L3_gnn_b1': 64.0,
     'L3_gnn_b2': 64.0,
     'L3_gnn_emb': 64.0,
     'L3_gnn_adaptW': 64.0}
    for name, (base, spread) in spreads.items():
        noise = np.random.default_rng([zlib.crc32(name.encode()), seed]).standard_normal(out[name].shape)
        drawn = base * np.exp(spread * noise) if base else spread * noise
        out[name] = jnp.asarray(drawn.astype(out[name].dtype))
    for name, factor in factors.items():
        out[name] = (out[name] * factor).astype(out[name].dtype)
    return out
```

```python
import concourse.bass as bass
from concourse import mybir
from concourse.alu_op_type import AluOpType as ALU
from contextlib import ExitStack
import math

F32, BF16, I32, I16 = mybir.dt.float32, mybir.dt.bfloat16, mybir.dt.int32, mybir.dt.int16
ACT = mybir.ActivationFunctionType
AX = mybir.AxisListType.X
ds = bass.ds

P = 128
CT = 5
NCH = 5
GT = CT * NCH
GE = GT * P
CE = CT * P
F = 48
H0 = 128
EA, EB = 32, 40
NTYPE, G = 119, 32
BW = H0 + G
HW = F + 1 + G
MW = F + 1
CUTOFF = 6.0
LN_EPS = 1e-5
BANK = 512
SLOT = [0, 1, 2, 0, 1]


class Plan:

    def __init__(self, n, e):
        self.N, self.E = n, e
        self.NT = e // P
        self.NG = e // GE
        assert self.NG * GE == e and self.NG <= P
        self.NB = -(-n // P)
        self.NP = self.NB * P
        self.NW = self.NP + P
        self.CB = max(k for k in range(1, 8) if self.NB % k == 0)
        self.NC = self.NB // self.CB


def links(eng, sem, base=0):
    count = [0]

    def link(ins):
        count[0] += 1
        ins.then_inc(sem, 1)
        eng.wait_ge(sem, base + count[0])
    return link


def bc(ap, shape):
    return ap.to_broadcast(shape)


def gnn(nc, a, out):
    pl = Plan(*a["size"])
    N, E, NT, NG, NB, NP, NW, CB, NC = pl.N, pl.E, pl.NT, pl.NG, pl.NB, pl.NP, pl.NW, pl.CB, pl.NC

    def dram(name, shape, dt=F32):
        return nc.dram_tensor(name, shape, dt, kind="Internal").ap()

    d = dict(
        ids16=dram("ids16", [2, E], I16),
        meta=dram("meta", [NG, 2], I32),
        atab=dram("atab", [NW, H0]),
        btab=dram("btab", [NP, BW]),
        esrc=dram("esrc", [P, NT, G]),
        y1=dram("y1", [NP, F]),
        y2=dram("y2", [NW, F]),
        htab=dram("htab", [NW, HW]),
        sum2=[dram(f"sum2_{k}", [NW, F]) for k in range(CT)],
        sum3=[dram(f"sum3_{k}", [NW, MW]) for k in range(CT)],
    )
    ctx = ExitStack()
    with ctx:
        def sb(name, shape, dt=F32):
            return ctx.enter_context(nc.sbuf_tensor(name, shape, dt))

        r = dict(
            x=sb("x", [P, NB, F]),
            acc=sb("acc", [P, NW]),
            iota_row=sb("iota_row", [P, P]),
            iota_row_bf=sb("iota_row_bf", [P, P], BF16),
            iota_p=sb("iota_p", [P, 1]),
            ident=sb("ident", [P, P]),
            before=sb("before", [P, P]),
            trash=sb("trash", [P, 1]),
            meta=sb("meta_row", [1, NG, 4], I32),
            basef=sb("basef", [P, NG]),
            outdeg=sb("outdeg", [P, NB]),
            indeg=sb("indeg", [P, NB]),
            ci=sb("ci", [P, NB]),
            dis=sb("dis", [P, NB]),
            mult=sb("mult", [P, NB]),
            uidx=sb("uidx", [P, NT], I32),
        )
        ps = ctx.enter_context(nc.psum_tensor("ps", [P, 8 * BANK], F32))
        prologue(nc, pl, a, d, r, ps)
        node_tables(nc, pl, a, d, r, ps)
        pass0(nc, pl, a, d, r, ps)
        epilogue0(nc, pl, a, d, r, ps)
        pass1(nc, pl, a, d, r, ps)
        epilogue1(nc, pl, a, d, r, ps)
        pass2(nc, pl, a, d, r, ps)
        epilogue2(nc, pl, a, d, r, ps)
        pass3(nc, pl, a, d, r, ps)
        epilogue3(nc, pl, a, d, r, ps, out)


class Stage:

    def __init__(self, nc, name):
        self.nc, self.name, self.ctx, self.sems = nc, name, ExitStack(), []

    def __enter__(self):
        self.ctx.__enter__()
        return self

    def __exit__(self, *e):
        self.ctx.__exit__(*e)
        self.nc.clear_and_free_semaphores(self.sems)
        self.nc.all_engine_barrier()

    def sb(self, name, shape, dt=F32):
        return self.ctx.enter_context(self.nc.sbuf_tensor(f"{self.name}_{name}", shape, dt))

    def sem(self, name):
        self.sems.append(self.nc.alloc_semaphore(f"{self.name}_{name}"))
        return self.sems[-1]

    def block(self):
        return self.ctx.enter_context(self.nc.Block())


def prologue(nc, pl, a, d, r, ps):
    NT, NG, E, NB = pl.NT, pl.NG, pl.E, pl.NB
    with Stage(nc, "pro") as s:
        flat = s.sb("flat", [P, 2, NT], I32)
        flat16 = s.sb("flat16", [P, 2, NT], I16)
        grp = s.sb("grp", [NG, GE], I32)
        lim = s.sb("lim", [NG, 2])
        rnd = s.sb("rnd", [NG, 2], I32)
        row = s.sb("row", [1, NG, 2], I32)
        rowf = s.sb("rowf", [1, 3, NG])
        bas = s.sb("bas", [P, NG, 2], I32)
        ones = s.sb("ones", [1, NG])
        flat_in, grp_in, x_in = s.sem("flat_in"), s.sem("grp_in"), s.sem("x_in")
        iotas, conv, lims, out16 = s.sem("iotas"), s.sem("conv"), s.sem("lims"), s.sem("out16")
        meta_out, row_in, self_v = s.sem("meta_out"), s.sem("row_in"), s.sem("self_v")
        block = s.block()

        @block.sync
        def _(sp):
            sp.dma_start(grp[:, :], a["dst"].rearrange("(g e) -> g e", e=GE)).then_inc(grp_in, 16)
            sp.dma_start(flat[:, 0, :], a["src"].rearrange("(q k) -> q k", q=P)).then_inc(flat_in, 16)
            sp.dma_start(flat[:, 1, :], a["dst"].rearrange("(q k) -> q k", q=P)).then_inc(flat_in, 16)
            sp.dma_start(r["x"][:, :, :], a["x"].rearrange("(b p) f -> p b f", p=P)).then_inc(x_in, 16)
            sp.dma_start(r["mult"][:, :], a["mult"]).then_inc(x_in, 16)
            sp.wait_ge(conv, 1)
            sp.dma_start(d["ids16"].rearrange("w (q k) -> q w k", q=P), flat16[:, :, :]).then_inc(out16, 16)
            sp.wait_ge(lims, 1)
            sp.dma_start(d["meta"], rnd[:, :]).then_inc(meta_out, 16)
            sp.wait_ge(meta_out, 16)
            sp.dma_start(row[:, :, :], d["meta"].rearrange("(o g) w -> o g w", o=1)).then_inc(row_in, 16)
            sp.dma_start(bas[:, :, :], d["meta"].rearrange("(o g) w -> o g w", o=1).to_broadcast([P, NG, 2])).then_inc(row_in, 16)
            sp.wait_ge(out16, 16)
            sp.wait_ge(x_in, 32)

        @block.gpsimd
        def _(pool):
            pool.iota(r["iota_row"][:, :], pattern=[[1, P]], base=0, channel_multiplier=0,
                      allow_small_or_imprecise_dtypes=True).then_inc(iotas, 1)
            pool.iota(r["iota_p"][:, :], pattern=[[1, 1]], base=0, channel_multiplier=1,
                      allow_small_or_imprecise_dtypes=True).then_inc(iotas, 1)
            pool.memset(r["acc"][:, :], 0.0)
            pool.memset(r["outdeg"][:, :], 0.0)
            pool.memset(r["indeg"][:, :], 0.0)

        @block.vector
        def _(dve):
            v = nc.vector
            link = links(dve, self_v)
            dve.wait_ge(grp_in, 16)
            link(v.tensor_reduce(lim[:, 0:1], grp[:, :], AX, ALU.min))
            link(v.tensor_reduce(lim[:, 1:2], grp[:, :], AX, ALU.max))
            link(v.tensor_tensor(lim[:, 1:2], lim[:, 1:2], lim[:, 0:1], ALU.subtract))
            link(v.tensor_copy(rnd[:, :], lim[:, :]))
            link(v.tensor_scalar(rnd[:, 1:2], rnd[:, 1:2], 7, None, ALU.arith_shift_right))
            link(v.tensor_copy(lim[:, 1:2], rnd[:, 1:2]))
            link(v.tensor_scalar(lim[:, 1:2], lim[:, 1:2], 1.0, None, ALU.add))
            v.tensor_copy(rnd[:, 1:2], lim[:, 1:2]).then_inc(lims, 1)
            dve.wait_ge(flat_in, 32)
            v.tensor_copy(flat16[:, :, :], flat[:, :, :]).then_inc(conv, 1)
            dve.wait_ge(iotas, 2)
            link(v.tensor_copy(r["iota_row_bf"][:, :], r["iota_row"][:, :]))
            link(v.tensor_scalar(r["ident"][:, :], r["iota_row"][:, :], r["iota_p"][:, :], None, ALU.is_equal))
            link(v.tensor_scalar(r["before"][:, :], r["iota_row"][:, :], r["iota_p"][:, :], None, ALU.is_lt))
            link(v.tensor_scalar(r["trash"][:, :], r["iota_p"][:, :], float(pl.NP), None, ALU.add))
            link(v.memset(ones[:, :], 1.0))
            dve.wait_ge(row_in, 32)
            link(v.tensor_copy(r["basef"][:, :], bas[:, :, 0]))
            link(v.tensor_copy(rowf[:, 0, :], row[:, :, 1]))
            link(v.tensor_tensor_scan(rowf[:, 1, :], ones[:, :], rowf[:, 0, :], 0.0, ALU.mult, ALU.add))
            link(v.tensor_tensor(rowf[:, 2, :], rowf[:, 1, :], rowf[:, 0, :], ALU.subtract))
            link(v.tensor_copy(r["meta"][:, :, 2], rowf[:, 2, :]))
            link(v.tensor_scalar(rowf[:, 0, :], rowf[:, 1, :], -1.0, None, ALU.add))
            link(v.tensor_copy(r["meta"][:, :, 3], rowf[:, 0, :]))
            link(v.tensor_copy(r["meta"][:, :, 0:2], row[:, :, :]))


def node_tables(nc, pl, a, d, r, ps):
    CB, NC = pl.CB, pl.NC
    CN = CB * P
    bank = ps[:, :].rearrange("p (b c) -> p b c", c=BANK)
    with Stage(nc, "tab") as s:
        xt = s.sb("xt", [F, CN])
        zb = s.sb("zb", [NTYPE, CN], I32)
        ohz = s.sb("ohz", [NTYPE, CN])
        w1 = s.sb("w1", [F, 2, H0])
        b1 = s.sb("b1", [P, H0])
        embt = s.sb("embt", [G, NTYPE])
        adt = s.sb("adt", [G, G])
        embc = s.sb("embc", [NTYPE, 2 * G])
        sta = s.sb("sta", [P, CB, H0])
        stb = s.sb("stb", [P, CB, BW])
        stp = s.sb("stp", [P, CB, G])
        zero = s.sb("zero", [P, H0])
        w_in, x_in, z_in = s.sem("w_in"), s.sem("x_in"), s.sem("z_in")
        embp, embr, oh, mm, sa, so = (s.sem(k) for k in ("embp", "embr", "oh", "mm", "sa", "so"))
        a_out, b_out, p_out, z_out, zs, stored = (s.sem(k) for k in ("a_out", "b_out", "p_out", "z_out", "zs", "stored"))
        block = s.block()

        @block.sync
        def _(sp):
            w1v = a["W1_0"].rearrange("(k f) h -> k f h", f=16)
            sp.dma_start(w1[:, :, :], a["W1_0"][0:2 * F, :].rearrange("(k f) h -> f k h", f=F)).then_inc(w_in, 16)
            sp.dma_start(b1[:, :], a["b1_0"].rearrange("(o h) -> o h", o=1).to_broadcast([P, H0])).then_inc(w_in, 16)
            sp.dma_start(embt[:, :], a["embT"]).then_inc(w_in, 16)
            sp.dma_start(adt[:, :], a["adaptWT"]).then_inc(w_in, 16)
            sp.dma_start(embc[:, 0:G], a["emb"]).then_inc(w_in, 16)
            sp.wait_ge(zs, 1)
            sp.dma_start(d["atab"][pl.NP:pl.NW, :], zero[:, :]).then_inc(z_out, 16)
            sp.dma_start(d["y2"][pl.NP:pl.NW, :], zero[:, 0:F]).then_inc(z_out, 16)
            sp.dma_start(d["htab"][pl.NP:pl.NW, :], zero[:, 0:HW]).then_inc(z_out, 16)
            with sp.Fori(0, NC) as c:
                sp.wait_ge(stored, c + 1)
                sp.nop(nofuse=True)
                sp.dma_start(xt[:, :], a["xT"][:, ds(c * CN, CN)]).then_inc(x_in, 16)
                sp.dma_start(zb[:, :], a["types"][:, ds(c * CN, CN)].to_broadcast([NTYPE, CN])).then_inc(z_in, 16)
                rows = ds(c * CN, CN)
                sp.wait_ge(sa, c + 1)
                sp.nop(nofuse=True)
                sp.dma_start(d["atab"][rows, :].rearrange("(b p) h -> p b h", p=P), sta[:, :, :]).then_inc(a_out, 16)
                sp.wait_ge(so, c + 1)
                sp.nop(nofuse=True)
                sp.dma_start(d["btab"][rows, :].rearrange("(b p) h -> p b h", p=P), stb[:, :, :]).then_inc(b_out, 16)
                sp.dma_start(d["htab"][rows, F + 1:HW].rearrange("(b p) h -> p b h", p=P), stp[:, :, :]).then_inc(p_out, 16)
                sp.wait_ge(a_out, (c + 1) * 16)
                sp.nop(nofuse=True)
                sp.wait_ge(b_out, (c + 1) * 16)
                sp.nop(nofuse=True)
                sp.wait_ge(p_out, (c + 1) * 16)
                sp.nop(nofuse=True)
                sp.sem_inc(stored, 1)
            sp.wait_ge(z_out, 48)

        @block.tensor
        def _(pe):
            t = nc.tensor
            pe.sem_inc(stored, 1)
            pe.wait_ge(w_in, 80)
            t.matmul(ps[0:NTYPE, 7 * BANK:7 * BANK + G], embt[:, :], adt[:, :], start=True, stop=True).then_inc(embp, 1)
            pe.wait_ge(embr, 1)
            with pe.Fori(0, NC) as c:
                pe.wait_ge(x_in, (c + 1) * 16)
                pe.wait_ge(oh, c + 1)
                pe.wait_ge(stored, c + 1)
                for j in range(CB):
                    t.matmul(bank[:, j, 0:2 * H0], xt[:, j * P:(j + 1) * P], w1[:, :, :].rearrange("f k h -> f (k h)"),
                             start=True, stop=True)
                    last = t.matmul(bank[:, j, 2 * H0:2 * H0 + 2 * G], ohz[:, j * P:(j + 1) * P], embc[:, :],
                                    start=True, stop=True)
                last.then_inc(mm, 1)

        @block.vector
        def _(dve):
            v = nc.vector
            v.memset(zero[:, :], 0.0).then_inc(zs, 1)
            dve.wait_ge(embp, 1)
            v.tensor_copy(embc[:, G:2 * G], ps[0:NTYPE, 7 * BANK:7 * BANK + G]).then_inc(embr, 1)
            with dve.Fori(0, NC) as c:
                dve.wait_ge(z_in, (c + 1) * 16)
                v.tensor_scalar(ohz[:, :], zb[:, :], r["iota_p"][0:NTYPE, :], None, ALU.is_equal).then_inc(oh, 1)
                dve.wait_ge(mm, c + 1)
                v.tensor_tensor(sta[:, :, :], bank[:, 0:CB, 0:H0], bc(b1[:, None, :], [P, CB, H0]), ALU.add).then_inc(sa, 1)

        @block.scalar
        def _(act):
            with act.Fori(0, NC) as c:
                act.wait_ge(sa, c + 1)
                nc.scalar.activation(stb[:, :, :], bank[:, 0:CB, H0:H0 + BW], ACT.Copy)
                nc.scalar.activation(stp[:, :, :], bank[:, 0:CB, 2 * H0 + G:2 * H0 + 2 * G], ACT.Copy).then_inc(so, 1)


def load_group(eng, pl, r, g):
    base = eng.value_load(r["meta"][0:1, ds(g, 1), 0], min_val=0, max_val=pl.NP - 1)
    rounds = eng.value_load(r["meta"][0:1, ds(g, 1), 1], min_val=1, max_val=pl.NB)
    before = eng.value_load(r["meta"][0:1, ds(g, 1), 2], min_val=0, max_val=pl.NG * pl.NB)
    return base, rounds, before


def last_round(eng, pl, r, g):
    return eng.value_load(r["meta"][0:1, ds(g, 1), 3], min_val=0, max_val=pl.NG * pl.NB)


def window_at(nc, pl, base, k):
    return nc.s_assert_within(base + k * P, 0, pl.NP - 1, 
                              skip_runtime_bounds_check_because="rounds end at the last destination")


def chunk_cols(c):
    return slice(c * CT, (c + 1) * CT)


def chunk_edges(c):
    return slice(c * CE, (c + 1) * CE)


def pass0(nc, pl, a, d, r, ps):
    NG, NB, NW, NT = pl.NG, pl.NB, pl.NW, pl.NT
    pre = [ps[:, k * 2 * BANK:k * 2 * BANK + CE] for k in range(2)]
    hacc = ps[:, 4 * BANK:4 * BANK + P]
    hsrc = ps[:, 5 * BANK:5 * BANK + NB]
    hdst = ps[:, 6 * BANK:6 * BANK + NB]
    acc = r["acc"]
    with Stage(nc, "l0") as s:
        sd = s.sb("sd", [P, GT, 2], I32)
        dstb = s.sb("dstb", [P, GE], I16)
        eat = s.sb("eat", [EA, GE])
        rows = s.sb("rows", [P, GT, BW])
        hid = s.sb("hid", [P, GT, H0])
        win = s.sb("win", [P, 2 * H0])
        wsel = s.sb("wsel", [EA, 2 * H0])
        oht = s.sb("oht", [P, 3, CE])
        ohe = s.sb("ohe", [P, 3, CT, P])
        nid = s.sb("nid", [P, 1])
        drel = s.sb("drel", [P, GT])
        dcolf = s.sb("dcolf", [P, GT])
        cnt = s.sb("cnt", [P, NCH])
        cnts = s.sb("cnts", [P, 1])
        nlo = s.sb("nlo", [P, 2])
        nidi = s.sb("nidi", [P, 2], I32)
        clo = s.sb("clo", [P, P])
        chi = s.sb("chi", [P, NB])
        slo = s.sb("slo", [P, GT], I32)
        shi = s.sb("shi", [P, GT], I32)
        slof = s.sb("slof", [P, GT], BF16)
        shif = s.sb("shif", [P, GT], BF16)
        hlo = s.sb("hlo", [P, 3, CT, P], BF16)
        hhi = s.sb("hhi", [P, 3, CT, NB], BF16)
        w_in, win_in = s.sem("w_in"), s.sem("win_in")
        sd_in, dstb_in, eat_in = ([s.sem(f"{k}{c}") for c in range(NCH)] for k in ("sd_in", "dstb_in", "eat_in"))
        gat, est = ([s.sem(f"{k}{c}") for c in range(NCH)] for k in ("gat", "est"))
        est_ok = s.sem("est_ok")
        wz = s.sem("wz")
        oht_ready, pre_ready = s.sem("oht_ready"), s.sem("pre_ready")
        pre_added = s.sem("pre_added")
        hid_ready = s.sem("hid_ready")
        hid_free = s.sem("hid_free")
        ohe_ready = s.sem("ohe_ready")
        acc_ready = s.sem("acc_ready")
        acc_added = s.sem("acc_added")
        cnt_ready = s.sem("cnt_ready")
        cnt_mm = s.sem("cnt_mm")
        hs_ready = s.sem("hs_ready")
        hs_used = s.sem("hs_used")
        hs_sum = s.sem("hs_sum")
        deg_added = s.sem("deg_added")
        ind_added = s.sem("ind_added")
        sd_used = s.sem("sd_used")
        win_used = s.sem("win_used")
        self_nid, self_rel, self_cnt, self_deg, self_sd = (s.sem(k) for k in ("self_nid", "self_rel", "self_cnt", "self_deg", "self_sd"))
        sum_ready = s.sem("sum_ready")
        block = s.block()

        @block.sync
        def _(sp):
            sp.dma_start(wsel[:, 0:H0], a["W1_0"][2 * F:2 * F + EA, :]).then_inc(w_in, 16)
            sp.sem_inc(est_ok, 5)
            with sp.Fori(0, NG) as g:
                base, rounds, before = load_group(sp, pl, r, g)
                for c in range(NCH):
                    t0 = g * GT + c * CT
                    sp.wait_ge(hid_ready, g * NCH + c + 1)
                    sp.nop(nofuse=True)
                    if c == 0:
                        sp.wait_ge(sd_used, g + 1)
                        sp.nop(nofuse=True)
                    sp.dma_start(sd[:, chunk_cols(c), :], a["sd"][:, ds(t0, CT), :]).then_inc(sd_in[c], 16)
                    sp.dma_start(dstb[:, chunk_edges(c)], d["ids16"][1:2, ds(t0 * P, CE)].to_broadcast([P, CE])).then_inc(dstb_in[c], 16)
                    sp.dma_start(eat[:, chunk_edges(c)], a["ea32T"][:, ds(t0 * P, CE)]).then_inc(eat_in[c], 16)
                with sp.Fori(0, rounds) as k:
                    w = before + k
                    sp.wait_ge(win_used, w + 1)
                    sp.nop(nofuse=True)
                    sp.dma_start(win[:, ds((w % 2) * H0, H0)], d["atab"][ds(window_at(nc, pl, base, k), P), :]).then_inc(win_in, 16)
                    sp.wait_ge(win_in, (w + 1) * 16)
                    sp.nop(nofuse=True)
                for c in range(NCH):
                    sp.wait_ge(gat[c], (g + 1) * 16 * CT)
                    sp.nop(nofuse=True)
                    sp.dma_start(d["esrc"][:, ds(g * GT + c * CT, CT), :], rows[:, chunk_cols(c), H0:BW]).then_inc(est[c], 16)
                    if c:
                        sp.wait_ge(est[c - 1], (g + 1) * 16)
                        sp.nop(nofuse=True)
                        sp.sem_inc(est_ok, 1)
                sp.wait_ge(est[NCH - 1], (g + 1) * 16)
                sp.nop(nofuse=True)
                sp.sem_inc(est_ok, 1)

        @block.gpsimd
        def _(pool):
            with pool.Fori(0, NG) as g:
                for c in range(NCH):
                    pool.wait_ge(sd_in[c], (g + 1) * 16)
                    pool.wait_ge(hid_ready, g * NCH + c + 1)
                    pool.wait_ge(est_ok, g * NCH + c + 1)
                    pool.nop(nofuse=True)
                    for t in range(c * CT, (c + 1) * CT):
                        pool.indirect_dma_start(rows[:, t, :], None, d["btab"], bass.IndirectOffsetOnAxis(
                            ap=sd[:, t, 0:1], axis=0)).then_inc(gat[c], 16)

        @block.vector
        def _(dve):
            v = nc.vector
            v.memset(wsel[:, H0:2 * H0], 0.0).then_inc(wz, 1)
            dve.sem_inc(pre_added, 2)
            dve.sem_inc(acc_added, 1)
            dve.sem_inc(self_rel, 1)
            dve.sem_inc(deg_added, 1)
            dve.sem_inc(ind_added, 1)
            dve.sem_inc(self_nid, 1)
            dve.sem_inc(sd_used, 1)
            with dve.Fori(0, NG) as g:
                base, rounds, before = load_group(dve, pl, r, g)
                dve.wait_ge(self_nid, before + g + 1)
                v.tensor_tensor(nid[:, :], r["basef"][:, ds(g, 1)], r["iota_p"][:, :], ALU.add).then_inc(self_nid, 1)

                with dve.Fori(0, rounds) as k:
                    w = before + k
                    n = w * NCH
                    dve.wait_ge(self_nid, w + g + 2)

                    def one_hot(c):
                        dve.wait_ge(dstb_in[c], (g + 1) * 16)
                        dve.wait_ge(self_cnt, w * 4 + 1)
                        dve.wait_ge(pre_ready, n + c + 1)
                        v.tensor_scalar(oht[:, SLOT[c], :], dstb[:, chunk_edges(c)], nid[:, :], 0.0, ALU.is_equal, ALU.add,
                                        accum_out=cnt[:, c:c + 1]).then_inc(oht_ready, 1)

                    one_hot(0)
                    for c in range(NCH):
                        if c + 1 < NCH:
                            one_hot(c + 1)
                        dve.wait_ge(gat[c], (g + 1) * 16 * CT)
                        dve.wait_ge(pre_ready, n + c + 3)
                        v.tensor_tensor(rows[:, chunk_cols(c), 0:H0], rows[:, chunk_cols(c), 0:H0],
                                        pre[c % 2].rearrange("p (t h) -> p t h", h=H0), ALU.add).then_inc(pre_added, 1)
                    dve.wait_ge(oht_ready, n + NCH)
                    v.tensor_reduce(cnts[:, :], cnt[:, :], AX, ALU.add).then_inc(self_cnt, 1)
                    v.tensor_copy(nidi[:, 0:1], nid[:, :]).then_inc(self_cnt, 1)
                    dve.wait_ge(self_cnt, w * 4 + 3)
                    v.tensor_scalar(nidi[:, 1:2], nidi[:, 0:1], 7, None, ALU.arith_shift_right).then_inc(self_cnt, 1)
                    dve.wait_ge(self_cnt, w * 4 + 4)
                    v.tensor_copy(nlo[:, 0:2], nidi[:, 0:2]).then_inc(self_cnt, 1)
                    dve.wait_ge(self_cnt, w * 4 + 5)
                    v.tensor_scalar(chi[:, :], r["iota_row"][:, 0:NB], nlo[:, 1:2], cnts[:, :], ALU.is_equal, ALU.mult)
                    v.scalar_tensor_tensor(nlo[:, 0:1], nlo[:, 1:2], -128.0, nlo[:, 0:1], ALU.mult, ALU.add).then_inc(self_deg, 1)
                    dve.wait_ge(self_deg, w + 1)
                    v.tensor_scalar(clo[:, :], r["iota_row"][:, :], nlo[:, 0:1], None, ALU.is_equal).then_inc(cnt_ready, 1)
                    v.tensor_scalar(nid[:, :], nid[:, :], float(P), None, ALU.add).then_inc(self_nid, 1)
                    dve.wait_ge(cnt_mm, w + 1)
                    v.tensor_tensor(r["indeg"][:, :], r["indeg"][:, :], hdst, ALU.add).then_inc(ind_added, 1)

                sl = links(dve, self_sd, g * 5)
                v.tensor_copy(dcolf[:, :], sd[:, :, 1]).then_inc(self_sd, 1)
                v.tensor_scalar(slo[:, :], sd[:, :, 0], 127, None, ALU.bitwise_and).then_inc(self_sd, 1)
                v.tensor_scalar(shi[:, :], sd[:, :, 0], 7, None, ALU.arith_shift_right).then_inc(self_sd, 1)
                dve.wait_ge(self_sd, g * 5 + 3)
                dve.wait_ge(self_rel, before + g + 1)
                v.tensor_scalar(drel[:, :], dcolf[:, :], r["basef"][:, ds(g, 1)], None, ALU.subtract).then_inc(self_rel, 1)
                v.tensor_copy(slof[:, :], slo[:, :]).then_inc(self_sd, 1)
                v.tensor_copy(shif[:, :], shi[:, :]).then_inc(self_sd, 1)
                dve.sem_inc(sd_used, 1)
                dve.wait_ge(self_sd, g * 5 + 5)

                def source_digits(c):
                    dve.wait_ge(hs_used, g * NCH + c + 1)
                    v.tensor_tensor(hlo[:, SLOT[c], :, :], bc(r["iota_row_bf"][:, None, :], [P, CT, P]),
                                    bc(slof[:, chunk_cols(c)].rearrange("p (t o) -> p t o", o=1), [P, CT, P]), ALU.is_equal)
                    v.tensor_tensor(hhi[:, SLOT[c], :, :], bc(r["iota_row_bf"][:, None, 0:NB], [P, CT, NB]),
                                    bc(shif[:, chunk_cols(c)].rearrange("p (t o) -> p t o", o=1), [P, CT, NB]), ALU.is_equal).then_inc(hs_ready, 1)

                for c in range(NCH):
                    source_digits(c)

                with dve.Fori(0, rounds) as k:
                    w = before + k
                    n = w * NCH
                    dve.wait_ge(self_rel, w + g + 2)
                    for c in range(NCH):
                        dve.wait_ge(hid_free, n + c + 3)
                        v.tensor_tensor(ohe[:, SLOT[c], :, :], bc(r["iota_row"][:, None, :], [P, CT, P]),
                                        bc(drel[:, chunk_cols(c)].rearrange("p (t o) -> p t o", o=1), [P, CT, P]), ALU.is_equal).then_inc(ohe_ready, 1)
                    dve.wait_ge(ohe_ready, n + NCH)
                    v.tensor_scalar(drel[:, :], drel[:, :], float(-P), None, ALU.add).then_inc(self_rel, 1)
                    dve.wait_ge(acc_ready, w + 1)
                    cols = acc[:, ds(window_at(nc, pl, base, k), P)]
                    v.tensor_tensor(cols, cols, hacc, ALU.add).then_inc(acc_added, 1)
                dve.wait_ge(hs_sum, g + 1)
                v.tensor_tensor(r["outdeg"][:, :], r["outdeg"][:, :], hsrc, ALU.add).then_inc(deg_added, 1)

        @block.tensor
        def _(pe):
            t = nc.tensor
            pe.sem_inc(pre_ready, 2)
            pe.sem_inc(hid_free, 5)
            pe.sem_inc(hs_used, 3)
            pe.sem_inc(win_used, 2)
            pe.sem_inc(self_cnt, 1)
            pe.wait_ge(w_in, 16)
            pe.wait_ge(wz, 1)
            with pe.Fori(0, NG) as g:
                base, rounds, before = load_group(pe, pl, r, g)
                with pe.Fori(0, rounds) as k:
                    w = before + k
                    n = w * NCH
                    window = win[:, ds((w % 2) * H0, H0)]
                    weights = wsel[:, ds(((k + (P - 1)) // P) * H0, H0)]
                    pe.wait_ge(win_in, (w + 1) * 16)
                    for c in range(NCH):
                        pe.wait_ge(oht_ready, n + c + 1)
                        pe.wait_ge(eat_in[c], (g + 1) * 16)
                        pe.wait_ge(pre_added, n + c + (1 if c else 2))
                        for j in range(CT):
                            o = pre[c % 2][:, j * P:(j + 1) * P]
                            t.matmul(o, oht[:, SLOT[c], j * P:(j + 1) * P], window, start=True, stop=False)
                            last = t.matmul(o, eat[:, c * CE + j * P:c * CE + (j + 1) * P], weights, start=False, stop=True)
                        last.then_inc(pre_ready, 1)
                    pe.wait_ge(cnt_ready, w + 1)
                    pe.wait_ge(ind_added, w + 1)
                    t.matmul(hdst, clo[:, :], chi[:, :], start=True, stop=True).then_inc(cnt_mm, 1)
                    pe.wait_ge(pre_ready, n + NCH + 2)
                    pe.sem_inc(win_used, 1)
                pe.wait_ge(deg_added, g + 1)
                for c in range(NCH):
                    pe.wait_ge(hs_ready, g * NCH + c + 1)
                    for j in range(CT):
                        last = t.matmul(hsrc, hlo[:, SLOT[c], j, :], hhi[:, SLOT[c], j, :],
                                        start=(c == 0 and j == 0), stop=(c == NCH - 1 and j == CT - 1))
                    last.then_inc(hs_used, 1)
                pe.wait_ge(hs_used, (g + 1) * NCH + 3)
                pe.sem_inc(hs_sum, 1)
                with pe.Fori(0, rounds) as k:
                    w = before + k
                    n = w * NCH
                    pe.wait_ge(acc_added, w + 1)
                    for c in range(NCH):
                        pe.wait_ge(hid_ready, 5 + g * NCH + c + 1)
                        pe.wait_ge(ohe_ready, n + c + 1)
                        for j in range(CT):
                            last = t.matmul(hacc, hid[:, c * CT + j, :], ohe[:, SLOT[c], j, :],
                                            start=(c == 0 and j == 0), stop=(c == NCH - 1 and j == CT - 1))
                        last.then_inc(hid_free, 1)
                    pe.wait_ge(hid_free, n + NCH + 5)
                    pe.sem_inc(acc_ready, 1)

        @block.scalar
        def _(act):
            act.sem_inc(hid_ready, 5)
            with act.Fori(0, NG) as g:
                base, rounds, before = load_group(act, pl, r, g)
                last = last_round(act, pl, r, g)
                for c in range(NCH):
                    act.wait_ge(pre_added, last * NCH + c + 3)
                    act.wait_ge(hid_free, before * NCH + c + 1)
                    nc.scalar.activation(hid[:, chunk_cols(c), :], rows[:, chunk_cols(c), 0:H0], ACT.Relu).then_inc(hid_ready, 1)


def norm_dve(nc, dve, link, x, t, m, var_ready, std_ready, nth):
    v = nc.vector
    NB = x.shape[1]
    link(v.tensor_reduce(m[:, :, 0], x[:, :, :], AX, ALU.add))
    link(v.tensor_scalar(m[:, :, 0], m[:, :, 0], 1.0 / F, None, ALU.mult))
    link(v.tensor_tensor(x[:, :, :], x[:, :, :], bc(m[:, :, 0:1], [P, NB, F]), ALU.subtract))
    link(v.tensor_tensor(t[:, :, 0:F], x[:, :, :], x[:, :, :], ALU.mult))
    link(v.tensor_reduce(m[:, :, 1], t[:, :, 0:F], AX, ALU.add))
    v.tensor_scalar(m[:, :, 1], m[:, :, 1], 1.0 / F, LN_EPS, ALU.mult, ALU.add).then_inc(var_ready, 1)
    dve.wait_ge(std_ready, nth)
    link(v.reciprocal(m[:, :, 1], m[:, :, 2]))
    link(v.tensor_tensor(x[:, :, :], x[:, :, :], bc(m[:, :, 1:2], [P, NB, F]), ALU.mult))


def norm_act(nc, act, m, var_ready, std_ready, nth):
    act.wait_ge(var_ready, nth)
    nc.scalar.activation(m[:, :, 2], m[:, :, 1], ACT.Sqrt).then_inc(std_ready, 1)


def by_node(table, NB):
    return table[0:NB * P, :].rearrange("(b p) f -> p b f", p=P)


def epilogue0(nc, pl, a, d, r, ps):
    NB, CB, NC = pl.NB, pl.CB, pl.NC
    CN = CB * P
    x = r["x"]
    with Stage(nc, "e0") as s:
        w2 = s.sb("w2", [H0, F])
        b2 = s.sb("b2", [P, F])
        st = s.sb("st", [P, CN])
        t = s.sb("t", [P, NB, F])
        m = s.sb("m", [P, NB, 3])
        q = s.sb("q", [P, NB, 3])
        out = ps[:, 0:CB * F].rearrange("p (b f) -> p b f", f=F)
        w_in, st_ready, mm, added, self_v = (s.sem(k) for k in ("w_in", "st_ready", "mm", "added", "self_v"))
        var_ready, std_ready, deg_ready, dstd_ready, y_ready, y_out = (s.sem(k) for k in ("var_ready", "std_ready", "deg_ready", "dstd_ready", "y_ready", "y_out"))
        block = s.block()

        @block.sync
        def _(sp):
            sp.dma_start(w2[:, :], a["W2_0"]).then_inc(w_in, 16)
            sp.dma_start(b2[:, :], a["b2_0"].rearrange("(o h) -> o h", o=1).to_broadcast([P, F])).then_inc(w_in, 16)
            sp.wait_ge(y_ready, 1)
            sp.dma_start(by_node(d["y1"], NB), t[:, :, :]).then_inc(y_out, 16)
            sp.wait_ge(y_out, 16)

        @block.scalar
        def _(act):
            with act.Fori(0, NC) as c:
                act.wait_ge(mm, c + 1)
                nc.scalar.activation(st[:, :], r["acc"][:, ds(c * CN, CN)], ACT.Copy).then_inc(st_ready, 1)
            act.wait_ge(deg_ready, 1)
            nc.scalar.activation(q[:, :, 2], q[:, :, 0], ACT.Sqrt).then_inc(dstd_ready, 1)
            norm_act(nc, act, m, var_ready, std_ready, 1)

        @block.tensor
        def _(pe):
            pe.sem_inc(mm, 1)
            pe.sem_inc(added, 1)
            pe.wait_ge(w_in, 32)
            with pe.Fori(0, NC) as c:
                pe.wait_ge(st_ready, c + 1)
                pe.wait_ge(added, c + 1)
                for j in range(CB):
                    last = nc.tensor.matmul(out[:, j, :], st[:, j * P:(j + 1) * P], w2[:, :], start=True, stop=True)
                last.then_inc(mm, 1)

        @block.vector
        def _(dve):
            v = nc.vector
            with dve.Fori(0, NC) as c:
                dve.wait_ge(mm, c + 2)
                xs = x[:, ds(c * CB, CB), :]
                v.tensor_tensor(xs, xs, out, ALU.add).then_inc(added, 1)
            link = links(dve, self_v)
            v.tensor_scalar(q[:, :, 0], r["outdeg"][:, :], 1.0, None, ALU.max).then_inc(deg_ready, 1)
            dve.wait_ge(w_in, 32)
            link(v.tensor_tensor(t[:, :, :], bc(r["indeg"][:, :].rearrange("p (b o) -> p b o", o=1), [P, NB, F]),
                                 bc(b2[:, None, :], [P, NB, F]), ALU.mult))
            dve.wait_ge(added, NC + 1)
            link(v.tensor_tensor(x[:, :, :], x[:, :, :], t[:, :, :], ALU.add))
            norm_dve(nc, dve, link, x, t, m, var_ready, std_ready, 1)
            dve.wait_ge(dstd_ready, 1)
            link(v.reciprocal(r["ci"][:, :], q[:, :, 2]))
            link(v.tensor_scalar(q[:, :, 1], r["outdeg"][:, :], 0.0, None, ALU.is_gt))
            link(v.tensor_tensor(r["dis"][:, :], r["ci"][:, :], q[:, :, 1], ALU.mult))
            v.tensor_tensor(t[:, :, :], x[:, :, :], bc(r["ci"][:, :].rearrange("p (b o) -> p b o", o=1), [P, NB, F]), ALU.mult).then_inc(y_ready, 1)

        @block.gpsimd
        def _(pool):
            pool.wait_ge(st_ready, NC)
            pool.memset(r["acc"][:, :], 0.0)


def pass1(nc, pl, a, d, r, ps):
    NG, NB, NW = pl.NG, pl.NB, pl.NW
    hacc = ps[0:F, 0:P]
    acc = r["acc"]
    ZW = (NB + 1) * MW
    with Stage(nc, "l1") as s:
        sd = s.sb("sd", [P, GT, 2], I32)
        rows = s.sb("rows", [P, GT, F])
        ohe = s.sb("ohe", [P, 3, CT, P])
        drel = s.sb("drel", [P, GT])
        dcolf = s.sb("dcolf", [P, GT])
        zero = s.sb("zero", [P, ZW])
        sd_in, gat = ([s.sem(f"{k}{c}") for c in range(NCH)] for k in ("sd_in", "gat"))
        zs, z_out = s.sem("zs"), s.sem("z_out")
        row_free = s.sem("row_free")
        ohe_ready, acc_ready = s.sem("ohe_ready"), s.sem("acc_ready")
        acc_added = s.sem("acc_added")
        sd_used = s.sem("sd_used")
        self_sd, self_rel = s.sem("self_sd"), s.sem("self_rel")
        block = s.block()

        @block.sync
        def _(sp):
            with sp.Fori(0, NG) as g:
                base, rounds, before = load_group(sp, pl, r, g)
                sp.wait_ge(sd_used, g + 1)
                sp.nop(nofuse=True)
                for c in range(NCH):
                    sp.wait_ge(row_free, before * NCH + c + 1)
                    sp.nop(nofuse=True)
                    sp.dma_start(sd[:, chunk_cols(c), :], a["sd"][:, ds(g * GT + c * CT, CT), :]).then_inc(sd_in[c], 16)

        @block.scalar
        def _(act):
            act.wait_ge(zs, 1)
            for k in range(CT):
                act.dma_start(d["sum2"][k].rearrange("(q k) f -> q (k f)", q=P), zero[:, 0:(NB + 1) * F]).then_inc(z_out, 16)
                act.dma_start(d["sum3"][k].rearrange("(q k) f -> q (k f)", q=P), zero[:, :]).then_inc(z_out, 16)
            act.wait_ge(z_out, 2 * CT * 16)

        @block.gpsimd
        def _(pool):
            with pool.Fori(0, NG) as g:
                base, rounds, before = load_group(pool, pl, r, g)
                for c in range(NCH):
                    pool.wait_ge(sd_in[c], (g + 1) * 16)
                    pool.wait_ge(row_free, before * NCH + c + 1)
                    pool.nop(nofuse=True)
                    for t in range(c * CT, (c + 1) * CT):
                        pool.indirect_dma_start(rows[:, t, :], None, d["y1"], bass.IndirectOffsetOnAxis(
                            ap=sd[:, t, 0:1], axis=0)).then_inc(gat[c], 16)

        @block.vector
        def _(dve):
            v = nc.vector
            v.memset(zero[:, :], 0.0).then_inc(zs, 1)
            dve.sem_inc(acc_added, 1)
            dve.sem_inc(self_rel, 1)
            dve.sem_inc(sd_used, 1)
            with dve.Fori(0, NG) as g:
                base, rounds, before = load_group(dve, pl, r, g)
                for c in range(NCH):
                    dve.wait_ge(sd_in[c], (g + 1) * 16)
                v.tensor_copy(dcolf[:, :], sd[:, :, 1]).then_inc(self_sd, 1)
                dve.wait_ge(self_sd, g + 1)
                dve.sem_inc(sd_used, 1)
                dve.wait_ge(self_rel, before + g + 1)
                v.tensor_scalar(drel[:, :], dcolf[:, :], r["basef"][:, ds(g, 1)], None, ALU.subtract).then_inc(self_rel, 1)
                with dve.Fori(0, rounds) as k:
                    w = before + k
                    n = w * NCH
                    dve.wait_ge(self_rel, w + g + 2)
                    for c in range(NCH):
                        dve.wait_ge(row_free, n + c + 3)
                        v.tensor_tensor(ohe[:, SLOT[c], :, :], bc(r["iota_row"][:, None, :], [P, CT, P]),
                                        bc(drel[:, chunk_cols(c)].rearrange("p (t o) -> p t o", o=1), [P, CT, P]), ALU.is_equal).then_inc(ohe_ready, 1)
                    dve.wait_ge(ohe_ready, n + NCH)
                    v.tensor_scalar(drel[:, :], drel[:, :], float(-P), None, ALU.add).then_inc(self_rel, 1)
                    dve.wait_ge(acc_ready, w + 1)
                    cols = acc[0:F, ds(window_at(nc, pl, base, k), P)]
                    v.tensor_tensor(cols, cols, hacc, ALU.add).then_inc(acc_added, 1)

        @block.tensor
        def _(pe):
            t = nc.tensor
            pe.sem_inc(row_free, 5)
            with pe.Fori(0, NG) as g:
                base, rounds, before = load_group(pe, pl, r, g)
                with pe.Fori(0, rounds) as k:
                    w = before + k
                    n = w * NCH
                    pe.wait_ge(acc_added, w + 1)
                    for c in range(NCH):
                        pe.wait_ge(gat[c], (g + 1) * 16 * CT)
                        pe.wait_ge(ohe_ready, n + c + 1)
                        for j in range(CT):
                            last = t.matmul(hacc, rows[:, c * CT + j, :], ohe[:, SLOT[c], j, :],
                                            start=(c == 0 and j == 0), stop=(c == NCH - 1 and j == CT - 1))
                        last.then_inc(row_free, 1)
                    pe.wait_ge(row_free, n + NCH + 5)
                    pe.sem_inc(acc_ready, 1)


def epilogue1(nc, pl, a, d, r, ps):
    NB, CB, NC = pl.NB, pl.CB, pl.NC
    CN = CB * P
    x = r["x"]
    with Stage(nc, "e1") as s:
        wt = s.sb("wt", [F, F])
        b = s.sb("b", [P, F])
        st = s.sb("st", [F, CN])
        xs = s.sb("xs", [P, CB, F])
        xst = s.sb("xst", [F, CN])
        t = s.sb("t", [P, NB, F])
        u = s.sb("u", [P, NB, F])
        m = s.sb("m", [P, NB, 3])
        q = s.sb("q", [P, NB, 4])
        xtp = ps[0:F, 0:CN]
        um = ps[:, 2 * BANK:2 * BANK + CB * F].rearrange("p (b f) -> p b f", f=F)
        vm = ps[:, 3 * BANK:3 * BANK + CB * F].rearrange("p (b f) -> p b f", f=F)
        w_in, xs_ready, st_ready, trans, xst_ready, mm, taken, self_v = (s.sem(k) for k in (
            "w_in", "xs_ready", "st_ready", "trans", "xst_ready", "mm", "taken", "self_v"))
        var_ready, std_ready, deg_ready, dstd_ready, y_ready, y_out = (s.sem(k) for k in ("var_ready", "std_ready", "deg_ready", "dstd_ready", "y_ready", "y_out"))
        block = s.block()

        @block.sync
        def _(sp):
            sp.dma_start(wt[:, :], a["WT_1"]).then_inc(w_in, 16)
            sp.dma_start(b[:, :], a["b_1"].rearrange("(o h) -> o h", o=1).to_broadcast([P, F])).then_inc(w_in, 16)
            sp.wait_ge(y_ready, 1)
            sp.dma_start(by_node(d["y2"], NB), t[:, :, :]).then_inc(y_out, 16)
            sp.wait_ge(y_out, 16)

        @block.scalar
        def _(act):
            act.wait_ge(deg_ready, 1)
            nc.scalar.activation(q[:, :, 2], q[:, :, 0], ACT.Sqrt).then_inc(dstd_ready, 1)
            with act.Fori(0, NC) as c:
                act.wait_ge(mm, c + 1)
                nc.scalar.activation(xs[:, :, :], x[:, ds(c * CB, CB), :], ACT.Copy).then_inc(xs_ready, 1)
                nc.scalar.activation(st[:, :], r["acc"][0:F, ds(c * CN, CN)], ACT.Copy).then_inc(st_ready, 1)
                act.wait_ge(trans, c + 1)
                nc.scalar.activation(xst[:, :], xtp, ACT.Copy).then_inc(xst_ready, 1)
            norm_act(nc, act, m, var_ready, std_ready, 1)

        @block.tensor
        def _(pe):
            pe.sem_inc(mm, 1)
            pe.sem_inc(taken, 1)
            pe.wait_ge(w_in, 32)
            with pe.Fori(0, NC) as c:
                pe.wait_ge(xs_ready, c + 1)
                pe.nop(nofuse=True)
                for j in range(CB):
                    last = nc.tensor.transpose(xtp[:, j * P:(j + 1) * P], xs[:, j, :], r["ident"][:, :])
                last.then_inc(trans, 1)
                pe.wait_ge(st_ready, c + 1)
                pe.wait_ge(taken, c + 1)
                for j in range(CB):
                    nc.tensor.matmul(um[:, j, :], st[:, j * P:(j + 1) * P], wt[:, :], start=True, stop=True)
                pe.wait_ge(xst_ready, c + 1)
                for j in range(CB):
                    last = nc.tensor.matmul(vm[:, j, :], xst[:, j * P:(j + 1) * P], wt[:, :], start=True, stop=True)
                last.then_inc(mm, 1)

        @block.vector
        def _(dve):
            v = nc.vector
            link = links(dve, self_v)
            v.tensor_scalar(q[:, :, 0], r["indeg"][:, :], 1.0, None, ALU.max).then_inc(deg_ready, 1)
            link(v.tensor_scalar(q[:, :, 3], r["indeg"][:, :], 0.0, None, ALU.is_le))
            dve.wait_ge(dstd_ready, 1)
            link(v.reciprocal(q[:, :, 1], q[:, :, 2]))
            with dve.Fori(0, NC) as c:
                dve.wait_ge(mm, c + 2)
                blocks = ds(c * CB, CB)
                v.tensor_tensor(t[:, blocks, :], um, bc(q[:, blocks, 1:2], [P, CB, F]), ALU.mult)
                v.tensor_tensor(u[:, blocks, :], vm, bc(q[:, blocks, 3:4], [P, CB, F]), ALU.mult).then_inc(taken, 1)
            dve.wait_ge(taken, NC + 1)
            link(v.tensor_tensor(t[:, :, :], t[:, :, :], u[:, :, :], ALU.add))
            link(v.tensor_tensor(t[:, :, :], t[:, :, :], bc(b[:, None, :], [P, NB, F]), ALU.add))
            link(v.scalar_tensor_tensor(x[:, :, :], t[:, :, :], 0.0, x[:, :, :], ALU.max, ALU.add))
            norm_dve(nc, dve, link, x, t, m, var_ready, std_ready, 1)
            v.tensor_tensor(t[:, :, :], x[:, :, :], bc(r["dis"][:, :].rearrange("p (b o) -> p b o", o=1), [P, NB, F]), ALU.mult).then_inc(y_ready, 1)


def pass2(nc, pl, a, d, r, ps):
    scatter_pass(nc, pl, a, d, r, ps, 2)


def pass3(nc, pl, a, d, r, ps):
    scatter_pass(nc, pl, a, d, r, ps, 3)


def scatter_pass(nc, pl, a, d, r, ps, layer):
    NG, NB, NT = pl.NG, pl.NB, pl.NT
    gated = layer == 3
    table, sums = (d["htab"], d["sum3"]) if gated else (d["y2"], d["sum2"])
    RW = HW if gated else F
    SW = MW if gated else F
    look = [ps[:, k * BANK:k * BANK + CT * RW].rearrange("p (t f) -> p t f", f=RW) for k in range(2)]
    comb = [ps[:, (2 + k) * BANK:(2 + k) * BANK + CT * SW].rearrange("p (t f) -> p t f", f=SW) for k in range(2)]
    zps = ps[0:F, 4 * BANK:6 * BANK].rearrange("p (k c) -> p k c", c=BANK)[:, :, 0:CE // 2]
    gps = ps[:, 6 * BANK:6 * BANK + CT * F].rearrange("p (t f) -> p t f", f=F)
    with Stage(nc, f"l{layer}") as s:
        sd = s.sb("sd", [P, GT, 2], I32)
        ids = [s.sb(f"ids{k}", [P, GE], I16) for k in range(2)]
        rows = s.sb("rows", [P, GT, RW])
        win = s.sb("win", [P, 2 * RW])
        oht = s.sb("oht", [P, 3, CE])
        same = s.sb("same", [P, 3, CE])
        nid = s.sb("nid", [P, 1])
        srcf = s.sb("srcf", [P, GT])
        msg = s.sb("msg", [P, GT, SW])
        uring = s.sb("uring", [P, GT], I32)
        sd_in, ids_in = ([s.sem(f"{k}{c}") for c in range(NCH)] for k in ("sd_in", "ids_in"))
        sc = [s.sem(f"sc{k}") for k in range(CT)]
        win_in, win_used = s.sem("win_in"), s.sem("win_used")
        oht_ready, look_ready = s.sem("oht_ready"), s.sem("look_ready")
        look_added = s.sem("look_added")
        rows_zero = s.sem("rows_zero")
        self_nid, self_sd, self_u = s.sem("self_nid"), s.sem("self_sd"), s.sem("self_u")
        same_ready = s.sem("same_ready")
        comb_done = s.sem("comb_done")
        comb_taken = s.sem("comb_taken")
        u_ready = s.sem("u_ready")
        scat_ok = s.sem("scat_ok")
        zt_set = s.sem("zt_set")
        zrow = s.sb("zrow", [P, SW])
        if gated:
            eat = s.sb("eat", [EB, GE])
            esr = s.sb("esr", [P, GT, G])
            w1 = s.sb("w1", [EB, F])
            w2 = s.sb("w2", [F + 1, F])
            b1 = s.sb("b1", [F, 1])
            sil = s.sb("sil", [F + 1, 3, CE])
            cw = s.sb("cw", [P, NT])
            cwt = s.sb("cwt", [P, NT])
            half_pi = s.sb("half_pi", [P, 1])
            prod = s.sb("prod", [P, CT, G])
            adapt = s.sb("adapt", [P, CT])
            gate = s.sb("gate", [P, CT, F])
            w_in = s.sem("w_in")
            ea_in, esr_in = ([s.sem(f"{k}{c}") for c in range(NCH)] for k in ("ea_in", "esr_in"))
            cwd, cws, ones_set, self_cw, self_m = (s.sem(k) for k in ("cwd", "cws", "ones_set", "self_cw", "self_m"))
            z_ready, sil_ready, gate_ready = s.sem("z_ready"), s.sem("sil_ready"), s.sem("gate_ready")
            gate_used = s.sem("gate_used")
            msg_ready = s.sem("msg_ready")
        else:
            prod = s.sb("prod", [P, CE])
            cnt = s.sb("cnt", [P, CT])
            fir = s.sb("fir", [P, CT])
            soff = s.sb("soff", [P, GT])
        block = s.block()

        @block.sync
        def _(sp):
            if gated:
                sp.dma_start(w1[:, :], a["W1T_3"]).then_inc(w_in, 16)
                sp.dma_start(w2[0:F, :], a["W2T_3"]).then_inc(w_in, 16)
                sp.dma_start(w2[F:F + 1, :], a["b2_3"].rearrange("(o f) -> o f", o=1)).then_inc(w_in, 16)
                sp.dma_start(b1[:, :], a["b1_3"].rearrange("(f o) -> f o", o=1)).then_inc(w_in, 16)
                sp.dma_start(cwt[:, :], a["dist"]).then_inc(w_in, 16)
            with sp.Fori(0, NG) as g:
                base, rounds, before = load_group(sp, pl, r, g)
                for c in range(NCH):
                    t0 = g * GT + c * CT
                    sp.wait_ge(comb_done, g * NCH + c + 1)
                    sp.nop(nofuse=True)
                    sp.dma_start(sd[:, chunk_cols(c), :], a["sd"][:, ds(t0, CT), :]).then_inc(sd_in[c], 16)
                    for k in range(2):
                        sp.dma_start(ids[k][:, chunk_edges(c)], d["ids16"][k:k + 1, ds(t0 * P, CE)].to_broadcast([P, CE])).then_inc(ids_in[c], 16)
                    if gated:
                        sp.dma_start(eat[:, chunk_edges(c)], a["ea40T"][:, ds(t0 * P, CE)]).then_inc(ea_in[c], 16)
                        sp.dma_start(esr[:, chunk_cols(c), :], d["esrc"][:, ds(t0, CT), :]).then_inc(esr_in[c], 16)
                with sp.Fori(0, rounds) as k:
                    w = before + k
                    sp.wait_ge(win_used, w + 1)
                    sp.nop(nofuse=True)
                    sp.dma_start(win[:, ds((w % 2) * RW, RW)], table[ds(window_at(nc, pl, base, k), P), :]).then_inc(win_in, 16)
                    sp.wait_ge(win_in, (w + 1) * 16)
                    sp.nop(nofuse=True)

        @block.gpsimd
        def _(pool):
            pool.sem_inc(scat_ok, 4)
            pool.wait_ge(zt_set, 1)
            for k in range(CT):
                pool.dma_start(sums[k][pl.NP:pl.NW, :], zrow[:, :]).then_inc(sc[k], 16)
            with pool.Fori(0, NG) as g:
                for c in range(NCH):
                    pool.wait_ge(comb_taken, g * NCH + c + 3)
                    pool.wait_ge(u_ready, g * NCH + c + 1)
                    for k in range(CT):
                        t = c * CT + k
                        pool.wait_ge(sc[k], (g * NCH + c + 1) * 16)
                        pool.nop(nofuse=True)
                        pool.indirect_dma_start(sums[k], bass.IndirectOffsetOnAxis(ap=uring[:, t:t + 1], axis=0),
                                                msg[:, t, :], None, compute_op=ALU.add).then_inc(sc[k], 16)
                    pool.sem_inc(scat_ok, 1)
            for k in range(CT):
                pool.wait_ge(sc[k], (NG * NCH + 1) * 16)

        @block.vector
        def _(dve):
            v = nc.vector
            dve.sem_inc(look_added, 2)
            dve.sem_inc(self_nid, 1)
            v.memset(zrow[:, :], 0.0).then_inc(zt_set, 1)
            if gated:
                dve.sem_inc(gate_used, 1)
                v.memset(half_pi[:, :], math.pi / 2)
                v.memset(sil[:, :, :], 1.0).then_inc(ones_set, 1)
                link = links(dve, self_cw)
                dve.wait_ge(w_in, 80)
                v.tensor_scalar(cw[:, :], cwt[:, :], CUTOFF, None, ALU.min).then_inc(cwd, 1)
                link(v.tensor_scalar(cwt[:, :], cwt[:, :], CUTOFF, 0.5, ALU.is_lt, ALU.mult))
                dve.wait_ge(cws, 1)
                link(v.scalar_tensor_tensor(cw[:, :], cw[:, :], 1.0, cwt[:, :], ALU.add, ALU.mult))
            with dve.Fori(0, NG) as g:
                base, rounds, before = load_group(dve, pl, r, g)
                dve.wait_ge(self_nid, before + g + 1)
                v.tensor_tensor(nid[:, :], r["basef"][:, ds(g, 1)], r["iota_p"][:, :], ALU.add).then_inc(self_nid, 1)
                dve.wait_ge(comb_done, (g + 1) * NCH)
                v.memset(rows[:, :, :], 0.0).then_inc(rows_zero, 1)
                with dve.Fori(0, rounds) as k:
                    w = before + k
                    n = w * NCH
                    dve.wait_ge(self_nid, w + g + 2)

                    def one_hot(c):
                        dve.wait_ge(ids_in[c], (g + 1) * 32)
                        dve.wait_ge(look_ready, n + c + 1)
                        v.tensor_scalar(oht[:, SLOT[c], :], ids[1][:, chunk_edges(c)], nid[:, :], None, ALU.is_equal).then_inc(oht_ready, 1)

                    one_hot(0)
                    dve.wait_ge(rows_zero, g + 1)
                    dve.wait_ge(look_added, n + 2)
                    for c in range(NCH):
                        if c + 1 < NCH:
                            one_hot(c + 1)
                        dve.wait_ge(look_ready, n + c + 3)
                        v.tensor_tensor(rows[:, chunk_cols(c), :], rows[:, chunk_cols(c), :], look[c % 2], ALU.add).then_inc(look_added, 1)
                    dve.wait_ge(oht_ready, n + NCH)
                    v.tensor_scalar(nid[:, :], nid[:, :], float(P), None, ALU.add).then_inc(self_nid, 1)
                for c in range(NCH):
                    dve.wait_ge(sd_in[c], (g + 1) * 16)
                v.tensor_copy(srcf[:, :], sd[:, :, 0]).then_inc(self_sd, 1)
                dve.wait_ge(self_sd, (g * 1 + 1) if gated else (g * 2 + 1))
                if not gated:
                    v.tensor_scalar(soff[:, :], srcf[:, :], r["trash"][:, :], None, ALU.subtract).then_inc(self_sd, 1)
                    dve.wait_ge(self_sd, g * 2 + 2)
                if gated:
                    dve.wait_ge(look_added, last_round(dve, pl, r, g) * NCH + NCH + 2)
                for c in range(NCH):
                    dve.wait_ge(comb_done, g * NCH + c + 3)
                    for j in range(CT):
                        t = c * CT + j
                        last = v.tensor_scalar(same[:, SLOT[c], j * P:(j + 1) * P], ids[0][:, t * P:(t + 1) * P],
                                               srcf[:, t:t + 1], None, ALU.is_equal)
                    last.then_inc(same_ready, 1)
                    if gated:
                        m = links(dve, self_m, (g * NCH + c) * 5)
                        mine = rows[:, chunk_cols(c), :]
                        dve.wait_ge(esr_in[c], (g + 1) * 16)
                        m(v.tensor_tensor(prod[:, :, :], esr[:, chunk_cols(c), :], mine[:, :, F + 1:HW], ALU.mult))
                        m(v.tensor_reduce(adapt[:, :], prod[:, :, :], AX, ALU.add))
                        dve.wait_ge(gate_ready, g * NCH + c + 1)
                        last = v.tensor_tensor(gate[:, :, :], gps, bc(adapt[:, :].rearrange("p (t o) -> p t o", o=1), [P, CT, F]), ALU.add)
                        m(last)
                        dve.sem_inc(gate_used, 1)
                        m(v.tensor_tensor(gate[:, :, :], gate[:, :, :], mine[:, :, 0:F], ALU.mult))
                        m(v.tensor_tensor(mine[:, :, 0:F], gate[:, :, :], bc(cw[:, ds(g * GT + c * CT, CT)].rearrange("p (t o) -> p t o", o=1), [P, CT, F]), ALU.mult))
                        dve.sem_inc(msg_ready, 1)
                    else:
                        u = links(dve, self_u, (g * NCH + c) * 4)
                        dve.wait_ge(same_ready, g * NCH + c + 1)
                        u(v.tensor_tensor(prod[:, :].rearrange("p (t e) -> p t e", e=P), same[:, SLOT[c], :].rearrange("p (t e) -> p t e", e=P),
                                          bc(r["before"][:, None, :], [P, CT, P]), ALU.mult))
                        u(v.tensor_reduce(cnt[:, :], prod[:, :].rearrange("p (t e) -> p t e", e=P), AX, ALU.add))
                        u(v.scalar_tensor_tensor(fir[:, :], cnt[:, :], 0.0, soff[:, chunk_cols(c)], ALU.is_equal, ALU.mult))
                        dve.wait_ge(scat_ok, g * NCH + c + 1)
                        u(v.tensor_scalar(uring[:, chunk_cols(c)], fir[:, :], r["trash"][:, :], None, ALU.add))
                        v.tensor_copy(r["uidx"][:, ds(g * GT + c * CT, CT)], uring[:, chunk_cols(c)]).then_inc(u_ready, 1)

        @block.tensor
        def _(pe):
            t = nc.tensor
            pe.sem_inc(look_ready, 2)
            pe.sem_inc(comb_done, 5)
            pe.sem_inc(win_used, 2)
            if gated:
                pe.wait_ge(w_in, 80)
                pe.wait_ge(ones_set, 1)
            with pe.Fori(0, NG) as g:
                base, rounds, before = load_group(pe, pl, r, g)
                with pe.Fori(0, rounds) as k:
                    w = before + k
                    n = w * NCH
                    window = win[:, ds((w % 2) * RW, RW)]
                    pe.wait_ge(win_in, (w + 1) * 16)
                    for c in range(NCH):
                        pe.wait_ge(oht_ready, n + c + 1)
                        pe.wait_ge(look_added, n + c + (1 if c else 2))
                        for j in range(CT):
                            last = t.matmul(look[c % 2][:, j, :], oht[:, SLOT[c], j * P:(j + 1) * P], window, start=True, stop=True)
                        last.then_inc(look_ready, 1)
                    pe.wait_ge(look_ready, n + NCH + 2)
                    pe.sem_inc(win_used, 1)

                last = last_round(pe, pl, r, g)

                def hidden(c):
                    m = g * NCH + c
                    pe.wait_ge(ea_in[c], (g + 1) * 16)
                    pe.wait_ge(sil_ready, m + 1)
                    pe.nop(nofuse=True)
                    for k in range(2):
                        last = t.matmul(zps[:, k, :], w1[:, :], eat[:, c * CE + k * CE // 2:c * CE + (k + 1) * CE // 2], start=True, stop=True)
                    last.then_inc(z_ready, 1)

                def gates(c):
                    m = g * NCH + c
                    pe.wait_ge(sil_ready, m + 2)
                    pe.wait_ge(gate_used, m + 1)
                    for j in range(CT):
                        last = t.matmul(gps[:, j, :], sil[:, SLOT[c], j * P:(j + 1) * P], w2[:, :], start=True, stop=True)
                    last.then_inc(gate_ready, 1)

                def combine(c):
                    m = g * NCH + c
                    pe.wait_ge(same_ready, m + 1)
                    if gated:
                        pe.wait_ge(msg_ready, m + 1)
                    else:
                        pe.wait_ge(look_added, last * NCH + c + 3)
                    pe.wait_ge(comb_taken, m + (1 if c else 2))
                    for j in range(CT):
                        done = t.matmul(comb[c % 2][:, j, :], same[:, SLOT[c], j * P:(j + 1) * P], rows[:, c * CT + j, 0:SW], start=True, stop=True)
                    done.then_inc(comb_done, 1)

                for i in range(NCH + 2 if gated else NCH):
                    if not gated:
                        combine(i)
                        continue
                    if i < NCH:
                        hidden(i)
                    if 1 <= i <= NCH:
                        gates(i - 1)
                    if i >= 2:
                        combine(i - 2)

        @block.scalar
        def _(act):
            act.sem_inc(comb_taken, 2)
            if gated:
                act.sem_inc(sil_ready, 1)
                act.wait_ge(cwd, 1)
                nc.scalar.activation(cw[:, :], cw[:, :], ACT.Sin, bias=half_pi[:, :], scale=-math.pi / CUTOFF).then_inc(cws, 1)
                act.wait_ge(ones_set, 1)

            with act.Fori(0, NG) as g:
                def silu(c):
                    act.wait_ge(z_ready, g * NCH + c + 1)
                    act.wait_ge(gate_ready, g * NCH + c - 1) if False else None
                    nc.scalar.activation(sil[0:F, SLOT[c], :].rearrange("p (k c) -> p k c", k=2), zps, ACT.Silu, bias=b1[:, :]).then_inc(sil_ready, 1)

                def take(c):
                    m = g * NCH + c
                    act.wait_ge(scat_ok, m + 1)
                    if gated:
                        nc.scalar.activation(uring[:, chunk_cols(c)], r["uidx"][:, ds(g * GT + c * CT, CT)], ACT.Copy).then_inc(u_ready, 1)
                    act.wait_ge(comb_done, 5 + m + 1)
                    nc.scalar.activation(msg[:, chunk_cols(c), :], comb[c % 2], ACT.Copy).then_inc(comb_taken, 1)

                for i in range(NCH + 2 if gated else NCH):
                    if not gated:
                        take(i)
                        continue
                    if i < NCH:
                        silu(i)
                    if i >= 2:
                        take(i - 2)


def sum_tables_sp(sp, tabs, bufs, t_in, free, NB):
    for k, tab in enumerate(tabs):
        if k >= 2:
            sp.wait_ge(free, k - 1)
        sp.dma_start(bufs[k % 2][:, :, :], by_node(tab, NB)).then_inc(t_in[k % 2], 16)


def epilogue2(nc, pl, a, d, r, ps):
    NB, CB, NC = pl.NB, pl.CB, pl.NC
    CN = CB * P
    x = r["x"]
    with Stage(nc, "e2") as s:
        wt = s.sb("wt", [F, F])
        b = s.sb("b", [P, F])
        xs = s.sb("xs", [P, CB, F])
        xst = s.sb("xst", [F, CN])
        bufs = [s.sb(f"buf{k}", [P, NB, F]) for k in range(2)]
        t = s.sb("t", [P, NB, F])
        ht = s.sb("ht", [P, NB, MW])
        m = s.sb("m", [P, NB, 3])
        xtp = ps[0:F, 0:CN]
        um = ps[:, 2 * BANK:2 * BANK + CB * F].rearrange("p (b f) -> p b f", f=F)
        t_in = [s.sem("t_in0"), s.sem("t_in1")]
        w_in, xs_ready, trans, xst_ready, mm, taken, self_v, free, agg = (s.sem(k) for k in (
            "w_in", "xs_ready", "trans", "xst_ready", "mm", "taken", "self_v", "free", "agg"))
        var_ready, std_ready, y_ready, y_out = (s.sem(k) for k in ("var_ready", "std_ready", "y_ready", "y_out"))
        block = s.block()

        @block.sync
        def _(sp):
            sp.dma_start(wt[:, :], a["WT_2"]).then_inc(w_in, 16)
            sp.dma_start(b[:, :], a["b_2"].rearrange("(o h) -> o h", o=1).to_broadcast([P, F])).then_inc(w_in, 16)
            sum_tables_sp(sp, d["sum2"], bufs, t_in, free, NB)
            sp.wait_ge(y_ready, 1)
            sp.dma_start(by_node(d["htab"][:, 0:MW], NB), ht[:, :, :]).then_inc(y_out, 16)
            sp.wait_ge(y_out, 16)

        @block.scalar
        def _(act):
            act.wait_ge(agg, 1)
            with act.Fori(0, NC) as c:
                act.wait_ge(trans, c + 1)
                nc.scalar.activation(xs[:, :, :], t[:, ds(c * CB, CB), :], ACT.Copy).then_inc(xs_ready, 1)
                act.wait_ge(trans, c + 2)
                act.wait_ge(mm, c + 1)
                nc.scalar.activation(xst[:, :], xtp, ACT.Copy).then_inc(xst_ready, 1)
            norm_act(nc, act, m, var_ready, std_ready, 1)

        @block.tensor
        def _(pe):
            pe.sem_inc(trans, 1)
            pe.sem_inc(mm, 1)
            pe.sem_inc(taken, 1)
            pe.wait_ge(w_in, 32)
            with pe.Fori(0, NC) as c:
                pe.wait_ge(xs_ready, c + 1)
                pe.nop(nofuse=True)
                for j in range(CB):
                    last = nc.tensor.transpose(xtp[:, j * P:(j + 1) * P], xs[:, j, :], r["ident"][:, :])
                last.then_inc(trans, 1)
                pe.wait_ge(taken, c + 1)
                pe.wait_ge(xst_ready, c + 1)
                for j in range(CB):
                    last = nc.tensor.matmul(um[:, j, :], xst[:, j * P:(j + 1) * P], wt[:, :], start=True, stop=True)
                last.then_inc(mm, 1)

        @block.vector
        def _(dve):
            v = nc.vector
            link = links(dve, self_v)
            for k in range(CT):
                dve.wait_ge(t_in[k % 2], 16 * (k // 2 + 1))
                if k == 0:
                    link(v.tensor_copy(ht[:, :, F:MW], r["mult"][:, :].rearrange("p (b o) -> p b o", o=1)))
                    v.tensor_copy(t[:, :, :], bufs[0][:, :, :]).then_inc(free, 1)
                else:
                    v.tensor_tensor(t[:, :, :], t[:, :, :], bufs[k % 2][:, :, :], ALU.add).then_inc(free, 1)
                dve.wait_ge(free, k + 1)
            v.tensor_tensor(t[:, :, :], t[:, :, :], bc(r["dis"][:, :].rearrange("p (b o) -> p b o", o=1), [P, NB, F]), ALU.mult).then_inc(agg, 1)
            with dve.Fori(0, NC) as c:
                dve.wait_ge(mm, c + 2)
                v.tensor_copy(bufs[0][:, ds(c * CB, CB), :], um).then_inc(taken, 1)
            dve.wait_ge(taken, NC + 1)
            dve.wait_ge(w_in, 32)
            link(v.tensor_tensor(bufs[0][:, :, :], bufs[0][:, :, :], bc(b[:, None, :], [P, NB, F]), ALU.add))
            link(v.scalar_tensor_tensor(x[:, :, :], bufs[0][:, :, :], 0.0, x[:, :, :], ALU.max, ALU.add))
            norm_dve(nc, dve, link, x, bufs[1], m, var_ready, std_ready, 1)
            dve.wait_ge(xs_ready, NC)
            v.tensor_tensor(ht[:, :, 0:F], x[:, :, :], bc(r["mult"][:, :].rearrange("p (b o) -> p b o", o=1), [P, NB, F]), ALU.mult).then_inc(y_ready, 1)


def epilogue3(nc, pl, a, d, r, ps, out):
    NB, N = pl.NB, pl.N
    x = r["x"]
    full = N // P
    with Stage(nc, "e3") as s:
        gam = s.sb("gam", [P, F])
        bet = s.sb("bet", [P, F])
        bufs = [s.sb(f"buf{k}", [P, NB, MW]) for k in range(2)]
        t = s.sb("t", [P, NB, MW])
        h = s.sb("h", [P, NB, F])
        m = s.sb("m", [P, NB, 3])
        t_in = [s.sem("t_in0"), s.sem("t_in1")]
        w_in, self_v, free, var_ready, std_ready, ready, o_out = (s.sem(k) for k in (
            "w_in", "self_v", "free", "var_ready", "std_ready", "ready", "o_out"))
        block = s.block()

        @block.sync
        def _(sp):
            sp.dma_start(gam[:, :], a["gamma"].rearrange("(o h) -> o h", o=1).to_broadcast([P, F])).then_inc(w_in, 16)
            sp.dma_start(bet[:, :], a["beta"].rearrange("(o h) -> o h", o=1).to_broadcast([P, F])).then_inc(w_in, 16)
            sum_tables_sp(sp, d["sum3"], bufs, t_in, free, NB)
            sp.wait_ge(ready, 1)
            sp.dma_start(out[0:full * P, :].rearrange("(b p) f -> p b f", p=P), x[:, 0:full, :]).then_inc(o_out, 16)
            if N > full * P:
                sp.dma_start(out[full * P:N, :], x[0:N - full * P, full, :]).then_inc(o_out, 16)
            sp.wait_ge(o_out, 32 if N > full * P else 16)

        @block.scalar
        def _(act):
            norm_act(nc, act, m, var_ready, std_ready, 1)
            norm_act(nc, act, m, var_ready, std_ready, 2)

        @block.vector
        def _(dve):
            v = nc.vector
            link = links(dve, self_v)
            for k in range(CT):
                dve.wait_ge(t_in[k % 2], 16 * (k // 2 + 1))
                if k == 0:
                    v.tensor_copy(t[:, :, :], bufs[0][:, :, :]).then_inc(free, 1)
                else:
                    v.tensor_tensor(t[:, :, :], t[:, :, :], bufs[k % 2][:, :, :], ALU.add).then_inc(free, 1)
                dve.wait_ge(free, k + 1)
            link(v.tensor_scalar(m[:, :, 0:1], t[:, :, F:MW], 1e-8, None, ALU.max))
            link(v.reciprocal(m[:, :, 1], m[:, :, 0]))
            link(v.tensor_tensor(h[:, :, :], t[:, :, 0:F], bc(m[:, :, 1:2], [P, NB, F]), ALU.mult))
            link(v.tensor_tensor(h[:, :, :], h[:, :, :], x[:, :, :], ALU.add))
            norm_dve(nc, dve, link, h, bufs[0], m, var_ready, std_ready, 1)
            dve.wait_ge(w_in, 32)
            link(v.tensor_tensor(h[:, :, :], h[:, :, :], bc(gam[:, None, :], [P, NB, F]), ALU.mult))
            link(v.tensor_tensor(h[:, :, :], h[:, :, :], bc(bet[:, None, :], [P, NB, F]), ALU.add))
            link(v.tensor_tensor(x[:, :, :], x[:, :, :], h[:, :, :], ALU.add))
            norm_dve(nc, dve, link, x, bufs[0], m, var_ready, std_ready, 2)
            dve.sem_inc(ready, 1)


def kernel(**inputs):
    import numpy as np
    import concourse.bacc as bacc
    from concourse.bass_utils import run_bass_kernel_spmd as run

    i = {k: np.asarray(v) for k, v in inputs.items()}
    n, e = i["x"].shape[0], i["src"].shape[0]
    pad = -(-n // P) * P - n
    x = np.pad(i["x"], ((0, pad), (0, 0)))
    src, dst = i["src"], i["dst"]
    arrays = dict(
        x=x, xT=x.T, src=src, dst=dst,
        sd=np.stack([src.reshape(-1, P).T, dst.reshape(-1, P).T], axis=-1),
        ea32T=i["edge_attr_32"].T, ea40T=i["edge_attr_40"].T,
        dist=i["edge_weight"].reshape(-1, P).T,
        types=np.pad(i["node_type_119"], (0, pad)).reshape(1, -1),
        mult=np.pad(i["node_vec"], (0, pad)).reshape(-1, P).T,
        W1_0=i["L0_gnn_W1"], b1_0=i["L0_gnn_b1"], W2_0=i["L0_gnn_W2"], b2_0=i["L0_gnn_b2"],
        WT_1=i["L1_gnn_W"].T, b_1=i["L1_gnn_b"], WT_2=i["L2_gnn_W"].T, b_2=i["L2_gnn_b"],
        W1T_3=i["L3_gnn_W1"].T, b1_3=i["L3_gnn_b1"], W2T_3=i["L3_gnn_W2"].T, b2_3=i["L3_gnn_b2"],
        emb=i["L3_gnn_emb"], embT=i["L3_gnn_emb"].T, adaptWT=i["L3_gnn_adaptW"].T,
        gamma=i["L3_gnn_gamma"], beta=i["L3_gnn_beta"],
    )
    arrays = {k: np.ascontiguousarray(v) for k, v in arrays.items()}
    nc = bacc.Bacc("TRN2", target_bir_lowering=False, num_devices=1)
    a = {k: nc.dram_tensor(f"in_{k}", v.shape, mybir.dt.from_np(v.dtype), kind="ExternalInput").ap()
         for k, v in arrays.items()}
    a["size"] = (n, e)
    out = nc.dram_tensor("out_0", (n, F), F32, kind="ExternalOutput").ap()
    gnn(nc, a, out)
    got = run(nc, [{f"in_{k}": v for k, v in arrays.items()}], core_ids=[0])
    return got.results[0]["out_0"]
```
